# Optimizing a Trainium2 kernel written in Bass

```python
import numpy as np
import jax
import jax.numpy as jnp

def _softmax(x, axis=-1):
    return jax.nn.softmax(x, axis=axis)

def _gelu(x):
    return jax.nn.gelu(x, approximate=True)

def _silu(x):
    return jax.nn.silu(x)

def _sigmoid(x):
    return jax.nn.sigmoid(x)

def _layernorm(x, axis=-1, eps=1e-05):
    m = jnp.mean(x, axis=axis, keepdims=True)
    v = jnp.var(x, axis=axis, keepdims=True)
    return (x - m) / jnp.sqrt(v + eps)

def _scatter_add(tgt, idx, src, axis=0):
    return tgt.at[idx].add(src)

def _segment_sum(src, seg, n):
    return jax.ops.segment_sum(src, seg, n)
kernel_name = 'mk_flamingo_gated_d1_seqx_r4_f8da83'

def setup_inputs(seed: int=0):
    np.random.seed(seed)
    _w = jnp.asarray

    def _rec_inputs():
        import jax
        import jax.numpy as jnp
        _rk = jax.random.key(seed)
        x = 7.22e-05 + 1 * jax.random.normal(jax.random.fold_in(_rk, 1), (64, 128, 256), jnp.float32)
        _lenS = 128 - jax.random.randint(jax.random.fold_in(_rk, 7), (64,), 0, max(1, 128 // 4) + 1, jnp.int32)
        _lenS2 = 128 - jax.random.randint(jax.random.fold_in(_rk, 8), (64,), 0, max(1, 128 // 4) + 1, jnp.int32)
        _ctx_1024P = jax.random.normal(jax.random.fold_in(_rk, 11), (64, 16, 256), jnp.float32)
        _ctx_1024c = jax.random.dirichlet(jax.random.fold_in(_rk, 511), 0.3 * jnp.ones((16,), jnp.float32), (64, 128))
        _ctx_1024t = jnp.einsum('bsk,bkd->bsd', _ctx_1024c, _ctx_1024P)
        _ctx_1024t = _ctx_1024t * jax.lax.rsqrt(jnp.mean(jnp.square(_ctx_1024t)) + 1e-12) * 0.953939
        ctx_1024 = 4.13588e-05 + 0.999923 * (_ctx_1024t + 0.3 * jax.random.normal(jax.random.fold_in(_rk, 611), (64, 128, 256), jnp.float32))
        _g = jax.random.normal(jax.random.fold_in(_rk, 9001), (2, 1), jnp.float32)
        _g = jnp.sign(_g) * jnp.maximum(jnp.abs(_g), 1.0) + (_g == 0) * 1.0
        g_xattn = _g[0]
        g_ffn = _g[1]
        return (x, ctx_1024, g_xattn, g_ffn)
    x, ctx_1024, g_xattn, g_ffn = _rec_inputs()

    def _L0_xattn_setup():
        import jax, jax.numpy as jnp
        import numpy as np
        NUM_HEADS = 16
        key = jax.random.key(seed)
        kq, kk, kv = jax.random.split(key, 3)
        B, S, E = (4, 512, 256)
        Q = jax.random.normal(kq, (B, S, E), dtype=jnp.float32)
        K = jax.random.normal(kk, (B, S, E), dtype=jnp.float32)
        V = jax.random.normal(kv, (B, S, E), dtype=jnp.float32)
        return {'Q': Q, 'K': K, 'V': V}
    _L0_xattn_all = _L0_xattn_setup()
    _L0_xattn_in = {k: v for k, v in _L0_xattn_all.items() if k in ()}
    del _L0_xattn_all

    def _L0_ffn_setup():
        import jax, jax.numpy as jnp
        import numpy as np
        N_BLOCKS = 16
        BLOCK = 64
        TOP_K = N_BLOCKS // 4
        key = jax.random.key(seed)
        ks = jax.random.split(key, 7)
        D, H = (256, 1024)
        s = lambda k, shape, scale: jax.random.normal(k, shape, dtype=jnp.float32) * scale
        return {'x': s(ks[0], (4, 1024, D), 1.0), 'w_router': s(ks[1], (D, N_BLOCKS), 0.03), 'b_router': s(ks[2], (N_BLOCKS,), 0.01), 'w1': s(ks[3], (H, D), 0.03), 'b1': s(ks[4], (H,), 0.01), 'w2': s(ks[5], (D, H), 0.03), 'b2': s(ks[6], (D,), 0.01)}
    _L0_ffn_all = _L0_ffn_setup()
    _L0_ffn_in = {k: v for k, v in _L0_ffn_all.items() if k in ('w_router', 'b_router', 'w1', 'b1', 'w2', 'b2')}
    del _L0_ffn_all
    return {'x': x, 'ctx_1024': ctx_1024, 'g_xattn': g_xattn, 'g_ffn': g_ffn, 'L0_ffn_w_router': _L0_ffn_in['w_router'], 'L0_ffn_b_router': _L0_ffn_in['b_router'], 'L0_ffn_w1': _L0_ffn_in['w1'], 'L0_ffn_b1': _L0_ffn_in['b1'], 'L0_ffn_w2': _L0_ffn_in['w2'], 'L0_ffn_b2': _L0_ffn_in['b2']}

def reference(x, ctx_1024, g_xattn, g_ffn, L0_ffn_w_router, L0_ffn_b_router, L0_ffn_w1, L0_ffn_b1, L0_ffn_w2, L0_ffn_b2):
    import jax
    import jax.numpy as jnp

    def _L0_xattn_ref(Q, K, V):
        import jax, jax.numpy as jnp
        import numpy as np
        NUM_HEADS = 16
        B, S, E = Q.shape
        H = NUM_HEADS
        d_k = E // H
        q = Q.reshape(B, S, H, d_k).transpose(0, 2, 1, 3)
        k = K.reshape(B, S, H, d_k).transpose(0, 2, 1, 3)
        v = V.reshape(B, S, H, d_k).transpose(0, 2, 1, 3)
        scale = 1.0 / np.sqrt(d_k).astype(np.float32)
        scores = jnp.einsum('bhqd,bhkd->bhqk', q, k) * scale
        causal_mask = jnp.tril(jnp.ones((S, S), dtype=bool))
        scores = jnp.where(causal_mask, scores, jnp.finfo(scores.dtype).min)
        attn = jax.nn.softmax(scores, axis=-1)
        out = jnp.einsum('bhqk,bhkd->bhqd', attn, v)
        return out.transpose(0, 2, 1, 3).reshape(B, S, E)

    def _L0_ffn_ref(x, w_router, b_router, w1, b1, w2, b2):
        import jax, jax.numpy as jnp
        import numpy as np
        N_BLOCKS = 16
        BLOCK = 64
        TOP_K = N_BLOCKS // 4
        orig_shape = x.shape
        D = orig_shape[-1]
        xf = x.reshape(-1, D)
        prob = jax.nn.softmax(xf @ w_router + b_router, axis=-1)
        _, idx = jax.lax.top_k(prob, TOP_K)
        mask = (idx[:, :, None] == jnp.arange(N_BLOCKS)[None, None, :]).any(axis=1)
        mask = mask.astype(x.dtype)
        w1b = w1.reshape(N_BLOCKS, BLOCK, D)
        b1b = b1.reshape(N_BLOCKS, BLOCK)
        w2b = jnp.transpose(w2.reshape(D, N_BLOCKS, BLOCK), (1, 2, 0))
        h = jax.nn.relu(jnp.einsum('nd,ebd->neb', xf, w1b) + b1b[None])
        y = jnp.einsum('neb,ebd,ne->nd', h, w2b, mask)
        y = y + b2[None, :]
        return y.reshape(orig_shape)
    x = x + jnp.tanh(g_xattn[0]) * _L0_xattn_ref(_layernorm(x, axis=-1), ctx_1024, ctx_1024)
    x = x + jnp.tanh(g_ffn[0]) * _L0_ffn_ref(_layernorm(x, axis=-1), L0_ffn_w_router, L0_ffn_b_router, L0_ffn_w1, L0_ffn_b1, L0_ffn_w2, L0_ffn_b2)
    return x

_drawn_inputs = setup_inputs


def setup_inputs(seed=0):
    import zlib

    import numpy as np

    out = dict(_drawn_inputs(seed))
    spreads = {}
    factors = {'L0_ffn_b_router': 3.368, 'L0_ffn_b1': 22.703, 'L0_ffn_b2': 7.084}
    for name, (base, spread) in spreads.items():
        noise = np.random.default_rng([zlib.crc32(name.encode()), seed]).standard_normal(out[name].shape)
        drawn = base * np.exp(spread * noise) if base else spread * noise
        out[name] = jnp.asarray(drawn.astype(out[name].dtype))
    for name, factor in factors.items():
        out[name] = (out[name] * factor).astype(out[name].dtype)
    return out
```

```python
from contextlib import ExitStack

import numpy as np

import concourse.bass as bass
from concourse import mybir

ALU = mybir.AluOpType
ACT = mybir.ActivationFunctionType
F32 = mybir.dt.float32
F32R = mybir.dt.float32r
BF16 = mybir.dt.bfloat16
AX_X = mybir.AxisListType.X

P = 128
HEADS = 16
SLOTS = 6
PARTS = 3
BANKS, BANK = 8, 512
GROUP = 4
PAIR = 2
PAD = 32
BLOCKS, TOP_K = 16, 4
LN_EPS = 1e-5
NEG = -(2.0 ** 126)
EXP_LOW = -87.33
TAKEN = -1.0e30
FILLER = 1.0e30

Q_SLOTS = {"high": slice(0, 3), "mid": slice(3, 6, 2), "low": slice(4, 5)}
K_SLOTS = {"high": slice(2, 5), "mid": slice(1, 6, 4), "low": slice(0, 1)}

LOAD_AHEAD = 5
FFN_LAG = 6


class Queue:

    def __init__(self):
        self.number = {}
        self.begin(None, None)

    def begin(self, engine, semaphore):
        self.engine, self.semaphore, self.count, self.waited = engine, semaphore, 0, {}

    def run(self, emit, *product):
        if product:
            self.count += 1
            self.number[product] = self.count
        if self.engine is not None:
            instruction = emit(self.engine)
            if product:
                instruction.then_inc(self.semaphore, 1)

    def wait(self, maker, *product):
        if self.engine is not None:
            self.wait_semaphore(maker.semaphore_of(), maker.number[product])

    def wait_semaphore(self, semaphore, value):
        if self.engine is not None and self.waited.get(semaphore.name, 0) < value:
            self.engine.wait_ge(semaphore, value)
            self.waited[semaphore.name] = value

    def settle(self):
        if self.count:
            self.wait_semaphore(self.done, self.count)

    def semaphore_of(self):
        return self.done


def build(nc, A_x, A_ctx, A_g_xattn, A_g_ffn, A_w_router, A_b_router, A_w1T, A_b1, A_w2T, A_b2, out):
    N, S, D = A_x.shape
    HID = A_w1T.shape[1]
    HD = D // HEADS
    BLOCK = HID // BLOCKS
    KC = D // P
    HC = HID // P
    STACK = SLOTS * HD
    GROUPS = N // GROUP
    HB = BANK // S
    TB = 2 * HB
    VW = HD + 1
    SCALE = float(HD) ** -0.5
    assert S == P and N % GROUP == 0 and HEADS // HB == 4 and STACK + PARTS <= P and HC == 8

    ctx = ExitStack()
    with ctx:
        def sb(name, shape, dt):
            return ctx.enter_context(nc.sbuf_tensor(name, shape, dt))

        def sem(name):
            return ctx.enter_context(nc.semaphore(name))

        banks = [ctx.enter_context(nc.psum_tensor(f"bank{i}", [P, BANK], F32)) for i in range(BANKS)]

        ident = sb("ident", [P, P], F32)
        ident16 = sb("ident16", [P, P], BF16)
        causal = sb("causal", [P, HB, S], BF16)
        half_power = sb("half_power", [P, 1], F32)
        gates = sb("gates", [P, 2], F32)
        tanh_g = sb("tanh_g", [P, 2], F32)
        b2_all = sb("b2_all", [P, D], F32)
        gated_b2 = sb("gated_b2", [P, D], F32)
        br_all = sb("br_all", [P, BLOCKS], F32)
        w_router = sb("w_router", [P, KC, PAD], F32)
        w_stage = sb("w_stage", [P, KC * HID], F32)
        w1_high = sb("w1_high", [P, KC, HID], F32R)
        w1_low = sb("w1_low", [P, KC, HID], F32R)
        w2_high = sb("w2_high", [P, HC, D], F32R)
        w2_low = sb("w2_low", [P, HC, D], F32R)
        b1_row, b1_rest = (w_stage[0:1, n * HID:(n + 1) * HID] for n in range(2))
        b1_parts = sb("b1_parts", [1, PARTS, HID], BF16)
        select = sb("select", [P, GROUP, HID], BF16)

        XS, CS, GS, VS = 8, 4, 12, 4
        x_in = sb("x_in", [P, XS, D], F32)
        c_in = sb("c_in", [P, CS, D], F32)
        stats1 = sb("stats1", [P, 2, 6], F32)
        mv1 = sb("mv1", [P, 2, 2], F32)
        ve1 = sb("ve1", [P, 2, 1], F32)
        rstd1 = sb("rstd1", [P, 2, 1], F32)
        qn = sb("qn", [P, 2, D], F32)
        q_rest = sb("q_rest", [P, 2, D], F32)
        k_rest = sb("k_rest", [P, 2, D], F32)
        q_stack = sb("q_stack", [P, 2, HEADS, SLOTS, HD], BF16)
        k_stack = sb("k_stack", [P, 2, HEADS, SLOTS, HD], BF16)
        v_ones = sb("v_ones", [P, VS, HEADS * VW + PAD - VW], F32)
        qT = sb("qT", [P, 2, HEADS * S], BF16)
        kT = sb("kT", [P, 2, HEADS * S], BF16)
        neg_max = sb("neg_max", [P, 2, HEADS], F32)
        max_rest = sb("max_rest", [P, 2, 2, HEADS], F32)
        max_parts = sb("max_parts", [P, 2, PARTS, HEADS], BF16)
        maxT = sb("maxT", [PARTS * HEADS, 2, S], BF16)
        weights = sb("weights", [P, 2, HEADS, S], F32)
        oT = sb("oT", [P, 2, BANK], F32)
        gain = sb("gain", [P, 2, 2, HEADS], F32)
        att = sb("att", [P, D], F32)
        x2 = sb("x2", [P, 2, D], F32)
        stats2 = sb("stats2", [P, 2, 6], F32)
        mv2 = sb("mv2", [P, 2, 2], F32)
        ve2 = sb("ve2", [P, 2, 1], F32)
        rstd2 = sb("rstd2", [P, 2, 1], F32)
        xn = sb("xn", [P, 2, D], F32)
        x2_b2 = sb("x2_b2", [P, GS, D], F32)

        xT = sb("xT", [P, KC, GROUP, S], F32)
        xT_high = sb("xT_high", [P, 2, KC, GROUP, S], F32R)
        xT_low = sb("xT_low", [P, 2, KC, GROUP, S], F32R)
        logitT = sb("logitT", [P, S], F32)
        logit = sb("logit", [P, GROUP, BLOCKS], F32)
        top8 = sb("top8", [P, GROUP, 8], F32)
        shifted = sb("shifted", [P, GROUP, BLOCKS], F32)
        below = sb("below", [P, GROUP, BLOCKS + 4], F32)
        chosen = sb("chosen", [P, GROUP, 8], F32)
        marked = sb("marked", [P, GROUP, BLOCKS + 4], F32)
        top_rest = sb("top_rest", [P, GROUP, TOP_K], F32)
        unused = sb("unused", [P, GROUP, PAD], BF16)
        unusedT = sb("unusedT", [P, 2, S], BF16)
        h_high = sb("h_high", [P, HC, GROUP * S], F32R)
        h_low = sb("h_low", [P, HC, GROUP * S], F32R)
        y_out = sb("y_out", [P, 2, 2, D], F32)

        pe, act, dve, pool = (Queue() for _ in range(4))
        for queue, name in ((pe, "pe_done"), (act, "act_done"), (dve, "dve_done"), (pool, "pool_done")):
            queue.done = sem(name)
        sync = Queue()
        sync.done = sem("sync_done")
        x_landed = [sem(f"x_landed{i}") for i in range(XS // PAIR)]
        c_landed = [sem(f"c_landed{i}") for i in range(CS // PAIR)]
        gates_landed = sem("gates_landed")
        small_landed = sem("small_landed")
        w_landed = sem("w_landed")
        b1_landed = sem("b1_landed")
        max_landed = [sem(f"max_landed{i}") for i in range(2)]
        y_stored = [sem(f"y_stored{i}") for i in range(2)]

        def landed(semaphores, b):
            turn, n = divmod(b // PAIR, len(semaphores))
            return semaphores[n], 16 * (turn + 1)

        def heads_view(ap):
            return ap.rearrange("p (h d) -> p h d", d=HD)

        def ffn_phase(i):
            g, phase = divmod(i - FFN_LAG, GROUP)
            return (g, phase) if 0 <= g < GROUPS else (None, None)

        def router_group(i):
            b = i - 2
            return b // GROUP if 0 <= b < N and b % GROUP == GROUP - 1 else None

        FIRST, LAST = -3, GROUP * (GROUPS - 1) + FFN_LAG + 3
        ITERATIONS = range(FIRST, LAST + 1)
        bank_of = {}

        def tensor_program(q):
            ring = []

            def take(name, *freed_by):
                n = len(ring)
                bank_of[name] = n % BANKS
                if n >= BANKS:
                    q.wait(*ring[n - BANKS])
                ring.append(freed_by)
                return banks[n % BANKS]

            def mm(*product, **args):
                q.run(lambda e: e.matmul(**args), *product)

            def tr(out_, in_, identity, *product):
                q.run(lambda e: e.transpose(out_, in_, identity), *product)

            def stacks_transposed(b):
                s = b % 2
                for side, stack, maker, name in (("q", q_stack, dve, "q low"), ("k", k_stack, pool, "k low")):
                    q.wait(maker, name, b)
                    for u in range(HEADS // TB):
                        evac = dve if side == "q" else act
                        bank = take((side + "T", b, u), evac, side + "T", b, u)[:].bitcast(BF16)
                        for h in range(TB):
                            last = (side + "T", b, u) if h == TB - 1 else ()
                            tr(bank[0:STACK, h * S:(h + 1) * S],
                               stack[:, s, u * TB + h].rearrange("p s d -> p (s d)"), ident16[:], *last)

            def scores(b):
                s = b % 2
                for u in range(HEADS // HB):
                    if u % 2 == 0:
                        q.wait(dve, "qT", b, u // 2)
                        q.wait(act, "kT", b, u // 2)
                    bank = take(("score", b, u), dve, "max", b, u)
                    mm(out=bank[:], lhsT=ident16[:], rhs=causal[:].rearrange("p h k -> p (h k)"),
                       start=True, stop=False)
                    for j in range(HB):
                        h = u * HB + j
                        cols = slice(h * S, (h + 1) * S)
                        last = ("score", b, u) if j == HB - 1 else ()
                        mm(*last, out=bank[:, j * S:(j + 1) * S], lhsT=qT[0:STACK, s, cols],
                           rhs=kT[0:STACK, s, cols], start=False, stop=j == HB - 1)

            def max_transposed(b):
                s = b % 2
                q.wait(dve, "max low", b)
                bank = take(("maxT", b), dve, "maxT", b)[:].bitcast(BF16)
                tr(bank[0:PARTS * HEADS, 0:S], max_parts[:, s].rearrange("p a h -> p (a h)"),
                   ident16[:], "maxT", b)

            def shifted_scores(b):
                s = b % 2
                q.wait_semaphore(max_landed[s], 16 * (b // 2 + 1))
                for u in range(HEADS // HB):
                    bank = take(("shifted", b, u), act, "exp", b, u)
                    for j in range(HB):
                        h = u * HB + j
                        cols = slice(h * S, (h + 1) * S)
                        last = ("shifted", b, u) if j == HB - 1 else ()
                        mm(*last, out=bank[:, j * S:(j + 1) * S], lhsT=kT[0:STACK + PARTS, s, cols],
                           rhs=qT[0:STACK + PARTS, s, cols], start=True, stop=True)

            def attention_out(b):
                s, vs = b % 2, b % VS
                bank = take(("oT", b), act, "oT", b)
                q.wait(pool, "v", b)
                for g in range(HEADS // HB):
                    q.wait(pool, "causal", b, g // 2)
                    for j in range(HB):
                        h = g * HB + j
                        last = ("oT", b) if h == HEADS - 1 else ()
                        mm(*last, out=bank[PAD * j:PAD * (j + 1), g * S:(g + 1) * S],
                           lhsT=v_ones[:, vs, h * VW:h * VW + PAD], rhs=weights[:, s, h, :],
                           start=True, stop=True, tile_position=(0, PAD * j))

            def out_transposed(b):
                s = b % 2
                bank = take(("o", b), dve, "att", b)
                q.wait(act, "oT", b)
                for g in range(HEADS // HB):
                    last = ("o", b) if g == HEADS // HB - 1 else ()
                    tr(bank[:, g * P:(g + 1) * P], oT[:, s, g * S:(g + 1) * S], ident[:], *last)

            def x_transposed(b):
                s = b % 2
                q.wait(dve, "xn", b)
                bank = take(("xT", b), act, "xT", b)
                for c in range(KC):
                    last = ("xT", b) if c == KC - 1 else ()
                    tr(bank[:, c * S:(c + 1) * S], xn[:, s, c * P:(c + 1) * P], ident[:], *last)

            def router_logits(g):
                bank = take(("logitT", g), act, "logitT", g)
                q.wait(act, "xT", g * GROUP + GROUP - 1)
                for c in range(KC):
                    for t in range(GROUP):
                        last = ("logitT", g) if c == KC - 1 and t == GROUP - 1 else ()
                        mm(*last, out=bank[PAD * t:PAD * (t + 1), 0:S], lhsT=w_router[:, c, :],
                           rhs=xT[:, c, t, :], start=c == 0, stop=c == KC - 1,
                           tile_position=(0, PAD * t))

            def logits_back(g):
                bank = take(("logit", g), dve, "logit", g)
                q.wait(act, "logitT", g)
                tr(bank[:, 0:P], logitT[:], ident[:], "logit", g)

            def unused_transposed(g):
                q.wait(dve, "unused", g)
                bank = take(("unusedT", g), dve, "unusedT", g)[:].bitcast(BF16)
                tr(bank[:, 0:S], unused[:].rearrange("p t e -> p (t e)"), ident16[:], "unusedT", g)

            def hidden(g, c):
                gs = g % 2
                cols = slice(c * P, (c + 1) * P)
                if c == 0:
                    q.wait(dve, "xT low", g * GROUP + GROUP - 1)
                    q.wait(dve, "w1 low")
                bank = take(("hidden", g, c), dve, "h low", g, c)
                for k in range(KC):
                    high, low = (t[:, gs, k].rearrange("p t s -> p (t s)") for t in (xT_high, xT_low))
                    mm(out=bank[:], lhsT=w1_high[:, k, cols], rhs=high, start=k == 0, stop=False)
                    mm(out=bank[:], lhsT=w1_high[:, k, cols], rhs=low, start=False, stop=False)
                    mm(out=bank[:], lhsT=w1_low[:, k, cols], rhs=high, start=False, stop=False)
                if c == 0:
                    q.wait(dve, "unusedT", g)
                    q.wait(pool, "select", GROUP - 1, 2)
                    q.wait_semaphore(b1_landed, 16 * GROUP)
                for t in range(GROUP):
                    last = ("hidden", g, c) if t == GROUP - 1 else ()
                    mm(*last, out=bank[:, t * S:(t + 1) * S], lhsT=select[:, t, cols],
                       rhs=unusedT[:, gs, :], start=False, stop=t == GROUP - 1)

            def ffn_out(g, t, half):
                if half == 0:
                    take(("ffn", g, t), dve, "y", g, t)
                bank = banks[bank_of[("ffn", g, t)]]
                toks = slice(t * S, (t + 1) * S)
                for c in range(half * HC // 2, (half + 1) * HC // 2):
                    q.wait(dve, "h low", g, c)
                    a, z = c == 0, c == HC - 1
                    last = ("ffn", g, t) if z else ()
                    mm(out=bank[:, 0:D], lhsT=h_high[:, c, toks], rhs=w2_high[:, c, :], start=a, stop=False)
                    mm(out=bank[:, 0:D], lhsT=h_high[:, c, toks], rhs=w2_low[:, c, :], start=False, stop=False)
                    mm(*last, out=bank[:, 0:D], lhsT=h_low[:, c, toks], rhs=w2_high[:, c, :],
                       start=False, stop=z)

            def ffn_piece(i, n):
                g, phase = ffn_phase(i)
                if g is None:
                    return
                if phase < 2:
                    hidden(g, phase * 4 + n)
                else:
                    ffn_out(g, (phase - 2) * 2 + n // 2, n % 2)

            q.wait(pool, "identities")
            for i in ITERATIONS:
                if 0 <= i < N:
                    if i == 0:
                        q.wait(pool, "causal mask")
                    scores(i)
                ffn_piece(i, 0)
                if 0 <= i - 2 < N:
                    x_transposed(i - 2)
                ffn_piece(i, 1)
                if 0 <= i < N:
                    max_transposed(i)
                if 0 <= i - 1 < N:
                    attention_out(i - 1)
                g = router_group(i)
                if g is not None:
                    if g == 0:
                        q.wait_semaphore(small_landed, 16 * (KC + 2))
                    router_logits(g)
                if 0 <= i + 1 < N:
                    stacks_transposed(i + 1)
                if g is not None:
                    logits_back(g)
                if 0 <= i - 1 < N:
                    out_transposed(i - 1)
                ffn_piece(i, 2)
                if g is not None:
                    unused_transposed(g)
                ffn_piece(i, 3)
                if 0 <= i < N:
                    shifted_scores(i)

        def scalar_program(q):
            def cast(stack, slots, source, s):
                n = len(range(*slots.indices(SLOTS)))
                q_in = heads_view(source).unsqueeze(2).to_broadcast([P, HEADS, n, HD])
                return lambda e: e.copy(stack[:, s, :, slots, :], q_in)

            def q_cast(b, part):
                s = b % 2
                if part == "high":
                    q.wait(dve, "qn", b)
                    if b >= 2:
                        q.wait(pe, "qT", b - 2, 1)
                    q.run(cast(q_stack, Q_SLOTS["high"], qn[:, s], s), "q high", b)
                else:
                    q.wait(dve, "q rest", b)
                    q.run(cast(q_stack, Q_SLOTS["mid"], q_rest[:, s], s), "q mid", b)

            def k_cast(b, part):
                s = b % 2
                if part == "high":
                    q.wait_semaphore(*landed(c_landed, b))
                    if b >= 2:
                        q.wait(pe, "kT", b - 2, 1)
                    q.run(cast(k_stack, K_SLOTS["high"], c_in[:, b % CS], s), "k high", b)
                else:
                    q.wait(pool, "k rest", b)
                    q.run(cast(k_stack, K_SLOTS["mid"], k_rest[:, s], s), "k mid", b)

            def exponentials(b):
                s = b % 2
                if b >= 2:
                    q.wait(pe, "oT", b - 2)
                for u in range(HEADS // HB):
                    q.wait(pe, "shifted", b, u)
                    bank = banks[bank_of[("shifted", b, u)]]
                    q.run(lambda e: e.activation(
                        weights[:, s, u * HB:(u + 1) * HB, :].rearrange("p h q -> p (h q)"), bank[:],
                        ACT.Exp, scale=SCALE), "exp", b, u)

            def relu_high(g, c):
                q.wait(pe, "hidden", g, c)
                if g >= 1:
                    q.wait(pe, "ffn", g - 1, GROUP - 1)
                bank = banks[bank_of[("hidden", g, c)]]
                q.run(lambda e: e.activation(h_high[:, c, :], bank[:], ACT.Relu), "h high", g, c)

            def ffn_piece(i, n):
                g, phase = ffn_phase(i)
                if g is not None and phase < 2:
                    relu_high(g, phase * 4 + n)

            q.wait_semaphore(gates_landed, 32)
            q.run(lambda e: e.activation(tanh_g[:], gates[:], ACT.Tanh), "tanh")
            for i in ITERATIONS:
                if 0 <= i - 1 < N:
                    exponentials(i - 1)
                if 0 <= i + 2 < N:
                    k_cast(i + 2, "high")
                ffn_piece(i, 0)
                if 0 <= i - 2 < N:
                    b = i - 2
                    g, t = divmod(b, GROUP)
                    q.wait(pe, "xT", b)
                    if b >= GROUP:
                        q.wait(dve, "xT low", b - 1)
                        q.wait(pe, "logitT", g - 1)
                    bank = banks[bank_of[("xT", b)]]
                    q.run(lambda e: e.copy(xT[:, :, t, :], bank[:, 0:D].rearrange("p (c s) -> p c s", s=S)),
                          "xT", b)
                if 0 <= i + 2 < N:
                    q_cast(i + 2, "high")
                    k_cast(i + 2, "mid")
                ffn_piece(i, 1)
                if 0 <= i - 1 < N:
                    b = i - 1
                    q.wait(pe, "oT", b)
                    bank = banks[bank_of[("oT", b)]]
                    q.run(lambda e: e.copy(oT[:, b % 2, :], bank[:]), "oT", b)
                g = router_group(i)
                if g is not None:
                    q.wait(pe, "logitT", g)
                    bank = banks[bank_of[("logitT", g)]]
                    q.run(lambda e: e.copy(logitT[:], bank[:, 0:S]), "logitT", g)
                if 0 <= i + 1 < N:
                    b = i + 1
                    for u in range(HEADS // TB):
                        q.wait(pe, "kT", b, u)
                        bank = banks[bank_of[("kT", b, u)]][0:STACK, :].bitcast(BF16)
                        q.run(lambda e: e.copy(kT[0:STACK, b % 2, u * TB * S:(u + 1) * TB * S], bank),
                              "kT", b, u)
                if 0 <= i + 2 < N:
                    q_cast(i + 2, "mid")
                ffn_piece(i, 2)
                ffn_piece(i, 3)

        def vector_program(q):
            def constants():
                q.run(lambda e: e.memset(w_router[:], 0.0), "w_router zero")
                q.run(lambda e: e.memset(half_power[:], -0.5), "half_power")
                for s in range(2):
                    q.run(lambda e: e.memset(kT[STACK:STACK + PARTS, s, :], 1.0))
                q.run(lambda e: e.memset(v_ones[:], 1.0), "v_ones")
                q.run(lambda e: e.memset(below[:, :, BLOCKS:], FILLER))
                q.run(lambda e: e.memset(chosen[:, :, TOP_K:], FILLER))
                q.run(lambda e: e.memset(unused[:], 0.0), "unused zero")
                q.wait(q, "unused zero")
                q.run(lambda e: e.memset(unused[:, :, BLOCKS:BLOCKS + PARTS], 1.0), "constants")
                q.wait(q, "constants")

            def stats_of(source, stats, mv, s, name, b):
                q.run(lambda e: e.bn_stats(stats[:, s, :], source), name + " stats", b)
                q.wait(q, name + " stats", b)
                q.run(lambda e: e.bn_aggr(mv[:, s, :], stats[:, s, :]), name + " mean", b)

            def layernorm_stats(b):
                q.wait_semaphore(*landed(x_landed, b))
                stats_of(x_in[:, b % XS, :], stats1, mv1, b % 2, "x", b)

            def normalised(b):
                s = b % 2
                q.wait(pool, "rstd1", b)
                q.run(lambda e: e.tensor_scalar(qn[:, s], x_in[:, b % XS, :], mv1[:, s, 0:1], rstd1[:, s],
                                                ALU.subtract, ALU.mult), "qn", b)

            def q_remainder(b):
                s = b % 2
                q.wait(act, "q high", b)
                q.run(lambda e: e.tensor_tensor(heads_view(q_rest[:, s]), heads_view(qn[:, s]),
                                                q_stack[:, s, :, 0, :], ALU.subtract), "q rest", b)

            def q_lowest(b):
                s = b % 2
                q.wait(act, "q mid", b)
                q.run(lambda e: e.tensor_tensor(q_stack[:, s, :, 4, :], heads_view(q_rest[:, s]),
                                                q_stack[:, s, :, 3, :], ALU.subtract), "q low", b)

            def row_maximum(b):
                s = b % 2
                for u in range(HEADS // HB):
                    q.wait(pe, "score", b, u)
                    bank = banks[bank_of[("score", b, u)]]
                    q.run(lambda e: e.tensor_reduce(
                        out=neg_max[:, s, u * HB:(u + 1) * HB], in_=bank[:].rearrange("p (h k) -> p h k", h=HB),
                        axis=AX_X, op=ALU.max, negate=True), "max", b, u)

            def maximum_parts(b):
                s = b % 2
                parts, rest = max_parts[:, s], max_rest[:, s]
                q.wait(q, "max", b, HEADS // HB - 1)
                if b >= 2:
                    q.wait(pe, "maxT", b - 2)
                q.run(lambda e: e.tensor_copy(parts[:, 0], neg_max[:, s]), "max high", b)
                q.wait(q, "max high", b)
                q.run(lambda e: e.tensor_tensor(rest[:, 0], neg_max[:, s], parts[:, 0], ALU.subtract), "max rest", b)
                q.wait(q, "max rest", b)
                q.run(lambda e: e.tensor_copy(parts[:, 1], rest[:, 0]), "max mid", b)
                q.wait(q, "max mid", b)
                q.run(lambda e: e.tensor_tensor(parts[:, 2], rest[:, 0], parts[:, 1], ALU.subtract), "max low", b)

            def maximum_rows(b):
                s = b % 2
                q.wait(pe, "maxT", b)
                if b >= 2:
                    q.wait_semaphore(max_landed[s], 16 * (b // 2))
                bank = banks[bank_of[("maxT", b)]][0:PARTS * HEADS, :].bitcast(BF16)
                q.run(lambda e: e.tensor_copy(maxT[:, s, :], bank[:, 0:S]), "maxT", b)

            def q_evacuated(b):
                s = b % 2
                if b >= 2:
                    q.wait(pe, "shifted", b - 2, HEADS // HB - 1)
                for u in range(HEADS // TB):
                    q.wait(pe, "qT", b, u)
                    bank = banks[bank_of[("qT", b, u)]][0:STACK, :].bitcast(BF16)
                    q.run(lambda e: e.tensor_copy(qT[0:STACK, s, u * TB * S:(u + 1) * TB * S], bank), "qT", b, u)

            def attention_added(b):
                s = b % 2
                q.wait(pe, "o", b)
                bank = banks[bank_of[("o", b)]][:].rearrange("p (h d) -> p h d", d=PAD)
                q.run(lambda e: e.reciprocal(gain[:, s, 0].unsqueeze(2), bank[:, :, HD:HD + 1]), "1/sum", b)
                q.wait(q, "1/sum", b)
                if b == 0:
                    q.wait(act, "tanh")
                q.run(lambda e: e.tensor_scalar(gain[:, s, 1], gain[:, s, 0], tanh_g[:, 0:1], None, ALU.mult),
                      "gain", b)
                q.wait(q, "gain", b)
                q.run(lambda e: e.tensor_tensor(
                    heads_view(att[:]), bank[:, :, 0:HD],
                    gain[:, s, 1].unsqueeze(2).to_broadcast([P, HEADS, HD]), ALU.mult), "att", b)
                q.wait(q, "att", b)
                if b >= 2:
                    q.wait(pool, "x2 b2", b - 2)
                q.run(lambda e: e.tensor_tensor(x2[:, s], att[:], x_in[:, b % XS, :], ALU.add), "x2", b)
                q.wait(q, "x2", b)
                stats_of(x2[:, s], stats2, mv2, s, "x2", b)

            def normalised_again(b):
                s = b % 2
                q.wait(pool, "rstd2", b)
                if b >= 2:
                    q.wait(pe, "xT", b - 2)
                q.run(lambda e: e.tensor_scalar(xn[:, s], x2[:, s], mv2[:, s, 0:1], rstd2[:, s],
                                                ALU.subtract, ALU.mult), "xn", b)

            def x_parts(b):
                g, t = divmod(b, GROUP)
                gs = g % 2
                q.wait(act, "xT", b)
                if g >= 2 and t == 0:
                    q.wait(pe, "hidden", g - 2, HC - 1)
                q.run(lambda e: e.tensor_copy(xT_high[:, gs, :, t, :], xT[:, :, t, :]), "xT high", b)
                q.wait(q, "xT high", b)
                q.run(lambda e: e.tensor_tensor(xT_low[:, gs, :, t, :], xT[:, :, t, :],
                                                xT_high[:, gs, :, t, :].bitcast(F32), ALU.subtract), "xT low", b)

            def relu_low(g, c):
                q.wait(act, "h high", g, c)
                bank = banks[bank_of[("hidden", g, c)]]
                q.run(lambda e: e.scalar_tensor_tensor(h_low[:, c, :], bank[:], 0.0, h_high[:, c, :].bitcast(F32),
                                                       ALU.max, ALU.subtract), "h low", g, c)

            def finished(g, t):
                b = g * GROUP + t
                pair = b // 2
                q.wait(pe, "ffn", g, t)
                if b % 2 == 0 and pair >= 2:
                    q.wait_semaphore(y_stored[pair % 2], 16 * (pair // 2))
                if b == 0:
                    q.wait(act, "tanh")
                q.wait(pool, "x2 b2", b)
                bank = banks[bank_of[("ffn", g, t)]]
                q.run(lambda e: e.scalar_tensor_tensor(y_out[:, pair % 2, b % 2, :], bank[:, 0:D], tanh_g[:, 1:2],
                                                       x2_b2[:, b % GS, :], ALU.mult, ALU.add), "y", g, t)

            def ffn_piece(i, n):
                g, phase = ffn_phase(i)
                if g is None:
                    return
                if phase < 2:
                    relu_low(g, phase * 4 + n)
                elif n % 2:
                    finished(g, (phase - 2) * 2 + n // 2)

            def route(g):
                q.wait(pe, "logit", g)
                bank = banks[bank_of[("logit", g)]][:, 0:P].rearrange("p (t e) -> p t e", e=PAD)
                if g == 0:
                    q.wait_semaphore(small_landed, 16 * (KC + 2))
                q.run(lambda e: e.tensor_tensor(logit[:], bank[:, :, 0:BLOCKS],
                                                br_all[:].unsqueeze(1).to_broadcast([P, GROUP, BLOCKS]), ALU.add),
                      "logit", g)
                q.wait(q, "logit", g)
                for t in range(GROUP):
                    q.run(lambda e: e.max(top8[:, t, :], logit[:, t, :]), "top8", g, t)
                q.wait(q, "top8", g, GROUP - 1)
                largest = top8[:, :, 0:1]
                q.run(lambda e: e.tensor_tensor(shifted[:], logit[:], largest.to_broadcast([P, GROUP, BLOCKS]),
                                                ALU.subtract), "shifted", g)
                q.run(lambda e: e.tensor_tensor(top_rest[:], top8[:, :, 0:TOP_K],
                                                largest.to_broadcast([P, GROUP, TOP_K]), ALU.subtract), "top rest", g)
                q.wait(q, "shifted", g)
                q.run(lambda e: e.tensor_scalar(below[:, :, 0:BLOCKS], shifted[:], EXP_LOW, None, ALU.max), "below", g)
                q.wait(q, "top rest", g)
                q.run(lambda e: e.tensor_scalar(chosen[:, :, 0:TOP_K], top_rest[:], EXP_LOW, None, ALU.max),
                      "chosen", g)
                q.wait(q, "chosen", g)
                for t in range(GROUP):
                    q.run(lambda e: e.match_replace(out=marked[:, t, :], in_to_replace=chosen[:, t, :],
                                                    in_values=below[:, t, :], imm_value=TAKEN), "marked", g, t)
                q.wait(q, "marked", g, GROUP - 1)
                q.run(lambda e: e.tensor_scalar(unused[:, :, 0:BLOCKS], marked[:, :, 0:BLOCKS], TAKEN, -1.0,
                                                ALU.is_equal, ALU.add), "unused", g)

            def split_weights(n):
                high, low, name = ((w1_high, w1_low, "w1"), (w2_high, w2_low, "w2"))[n]
                flat_high, flat_low = (t[:].rearrange("p c n -> p (c n)") for t in (high, low))
                q.wait_semaphore(w_landed, 16 * (n + 1))
                q.run(lambda e: e.tensor_copy(flat_high, w_stage[:]), name + " high")
                q.wait(q, name + " high")
                q.run(lambda e: e.tensor_tensor(flat_low, w_stage[:], flat_high.bitcast(F32), ALU.subtract),
                      name + " low")

            def split_b1():
                parts = b1_parts[:]
                q.wait_semaphore(w_landed, 16 * 3)
                q.run(lambda e: e.tensor_copy(parts[:, 0], b1_row), "b1 high")
                q.wait(q, "b1 high")
                q.run(lambda e: e.tensor_tensor(b1_rest, b1_row, parts[:, 0], ALU.subtract), "b1 rest")
                q.wait(q, "b1 rest")
                q.run(lambda e: e.tensor_copy(parts[:, 1], b1_rest), "b1 mid")
                q.wait(q, "b1 mid")
                q.run(lambda e: e.tensor_tensor(parts[:, 2], b1_rest, parts[:, 1], ALU.subtract), "b1 parts")

            constants()
            for b in range(min(1, N)):
                layernorm_stats(b)
            for i in ITERATIONS:
                if 0 <= i + 3 < N and i + 3 > 0:
                    layernorm_stats(i + 3)
                if 0 <= i + 2 < N:
                    normalised(i + 2)
                if 0 <= i < N:
                    row_maximum(i)
                    maximum_parts(i)
                if 0 <= i - 2 < N:
                    x_parts(i - 2)
                ffn_piece(i, 0)
                if 0 <= i + 2 < N:
                    q_remainder(i + 2)
                ffn_piece(i, 1)
                if 0 <= i < N:
                    maximum_rows(i)
                if 0 <= i + 1 < N:
                    q_evacuated(i + 1)
                g = router_group(i)
                if g is not None:
                    route(g)
                if 0 <= i - 1 < N:
                    attention_added(i - 1)
                if 0 <= i + 2 < N:
                    q_lowest(i + 2)
                ffn_piece(i, 2)
                if 0 <= i - 1 < N:
                    normalised_again(i - 1)
                if g is not None:
                    q.wait(pe, "unusedT", g)
                    bank = banks[bank_of[("unusedT", g)]][:].bitcast(BF16)
                    q.run(lambda e: e.tensor_copy(unusedT[:, g % 2, :], bank[:, 0:S]), "unusedT", g)
                ffn_piece(i, 3)
                if i == 1:
                    q.wait_semaphore(small_landed, 16 * (KC + 2))
                    q.wait(act, "tanh")
                    q.run(lambda e: e.tensor_scalar(gated_b2[:], b2_all[:], tanh_g[:, 1:2], None, ALU.mult), "gated b2")
                if i in (2, 3):
                    split_weights(i - 2)
                if i == 4:
                    split_b1()

        def pool_program(q):
            def rstd(mv, ve, result, s, maker_name, name, b):
                q.wait(dve, maker_name, b)
                q.run(lambda e: e.tensor_scalar(ve[:, s], mv[:, s, 1:2], LN_EPS, None, ALU.add), name + " ve", b)
                q.wait(q, name + " ve", b)
                q.run(lambda e: e.tensor_tensor(result[:, s], ve[:, s], half_power[:], ALU.pow), name, b)

            def k_remainder(b):
                s = b % 2
                q.wait(act, "k high", b)
                q.run(lambda e: e.tensor_tensor(heads_view(k_rest[:, s]), heads_view(c_in[:, b % CS, :]),
                                                k_stack[:, s, :, 2, :], ALU.subtract), "k rest", b)

            def k_lowest(b):
                s = b % 2
                q.wait(act, "k mid", b)
                q.run(lambda e: e.tensor_tensor(k_stack[:, s, :, 0, :], heads_view(k_rest[:, s]),
                                                k_stack[:, s, :, 1, :], ALU.subtract), "k low", b)

            def values(b):
                q.wait_semaphore(*landed(c_landed, b))
                if b == 0:
                    q.wait(dve, "v_ones")
                if b >= VS:
                    q.wait(pe, "oT", b - VS)
                v = v_ones[:, b % VS, 0:HEADS * VW].rearrange("p (h w) -> p h w", w=VW)
                q.run(lambda e: e.tensor_copy(v[:, :, 0:HD], heads_view(c_in[:, b % CS, :])), "v", b)

            def causal_weights(b):
                s = b % 2
                for half in range(2):
                    w = weights[:, s, half * 2 * HB:(half + 1) * 2 * HB, :]
                    q.wait(act, "exp", b, half * 2 + 1)
                    q.run(lambda e: e.affine_select(out=w, in_=w, compare_op=ALU.is_ge, fill=0.0, base=0,
                                                    pattern=[[0, 2 * HB], [1, S]], channel_multiplier=-1),
                          "causal", b, half)

            def identity(tile, name):
                q.run(lambda e: e.memset(tile[:], 0.0), name + " zero")
                q.wait(q, name + " zero")
                q.run(lambda e: e.affine_select(out=tile[:], in_=tile[:], compare_op=ALU.not_equal, fill=1.0,
                                                base=0, pattern=[[-1, P]], channel_multiplier=1), name)

            def causal_mask():
                q.run(lambda e: e.memset(causal[:], 0.0), "causal zero")
                q.wait(q, "causal zero")
                q.run(lambda e: e.affine_select(out=causal[:], in_=causal[:], compare_op=ALU.is_ge, fill=NEG,
                                                base=0, pattern=[[0, HB], [-1, S]], channel_multiplier=1),
                      "causal mask")

            def select_table(t):
                rows = select[PAD * t:PAD * (t + 1), t, :]
                q.run(lambda e: e.memset(rows, -NEG), "select", t, 0)
                q.wait(q, "select", t, 0)
                q.run(lambda e: e.affine_select(out=rows, in_=rows, compare_op=ALU.is_ge, fill=0.0, base=0,
                                                pattern=[[1, HID]], channel_multiplier=-BLOCK), "select", t, 1)
                q.wait(q, "select", t, 1)
                q.run(lambda e: e.affine_select(out=rows, in_=rows, compare_op=ALU.is_ge, fill=0.0,
                                                base=BLOCK - 1, pattern=[[-1, HID]], channel_multiplier=BLOCK),
                      "select", t, 2)

            identity(ident16, "ident16")
            identity(ident, "identities")
            for i in ITERATIONS:
                if 0 <= i - 1 < N:
                    causal_weights(i - 1)
                if 0 <= i + 3 < N:
                    if i + 3 == 0:
                        q.wait(dve, "half_power")
                    rstd(mv1, ve1, rstd1, (i + 3) % 2, "x mean", "rstd1", i + 3)
                if 0 <= i + 2 < N:
                    k_remainder(i + 2)
                    values(i + 2)
                    k_lowest(i + 2)
                if 0 <= i - 1 < N:
                    b = i - 1
                    rstd(mv2, ve2, rstd2, b % 2, "x2 mean", "rstd2", b)
                    if b == 0:
                        q.wait(dve, "gated b2")
                    if b >= GS:
                        q.wait(dve, "y", *divmod(b - GS, GROUP))
                    q.run(lambda e: e.tensor_tensor(x2_b2[:, b % GS, :], x2[:, b % 2], gated_b2[:], ALU.add),
                          "x2 b2", b)
                if i == -1:
                    causal_mask()
                if i == 0:
                    q.run(lambda e: e.memset(select[:], 0.0), "select zero")
                    q.wait(q, "select zero")
                if 0 <= i < GROUP:
                    q.settle()
                    select_table(i)
                    q.settle()

        def sync_program(q):
            def dma(semaphore, dst, src):
                q.run(lambda e: e.dma_start(dst, src).then_inc(semaphore, 16))

            def load(n):
                tiles = slice(n * PAIR, (n + 1) * PAIR)
                xs, cs = n % (XS // PAIR), n % (CS // PAIR)
                if n * PAIR >= CS:
                    b = n * PAIR - CS + PAIR - 1
                    q.wait(pool, "k rest", b)
                    q.wait(pool, "v", b)
                dma(c_landed[cs], c_in[:, cs * PAIR:(cs + 1) * PAIR, :], A_ctx[tiles].rearrange("b p d -> p b d"))
                if n * PAIR >= XS:
                    q.wait(dve, "x2", n * PAIR - XS + PAIR - 1)
                dma(x_landed[xs], x_in[:, xs * PAIR:(xs + 1) * PAIR, :], A_x[tiles].rearrange("b p d -> p b d"))

            load(0)
            dma(gates_landed, gates[:, 0:1], A_g_xattn.partition_broadcast(P))
            dma(gates_landed, gates[:, 1:2], A_g_ffn.partition_broadcast(P))
            dma(small_landed, b2_all[:], A_b2.partition_broadcast(P))
            dma(small_landed, br_all[:], A_b_router.partition_broadcast(P))
            q.wait(dve, "w_router zero")
            for c in range(KC):
                dma(small_landed, w_router[:, c, 0:BLOCKS], A_w_router[c * P:(c + 1) * P, :])
            load(1)
            dma(w_landed, w_stage[:].rearrange("p (c n) -> p c n", c=KC), A_w1T.rearrange("(c p) n -> p c n", p=P))
            for i in ITERATIONS:
                b = i + LOAD_AHEAD
                if b >= 2 * PAIR and b % PAIR == 0 and b < N:
                    load(b // PAIR)
                if i == 3:
                    q.wait(dve, "w1 low")
                    dma(w_landed, w_stage[:].rearrange("p (c n) -> p c n", c=HC),
                        A_w2T.rearrange("(c p) n -> p c n", p=P))
                if i == 4:
                    q.wait(dve, "w2 low")
                    dma(w_landed, b1_row, A_b1.rearrange("(o n) -> o n", o=1))
                if 0 <= i < N:
                    q.wait(dve, "maxT", i)
                    dma(max_landed[i % 2], qT[STACK:STACK + PARTS, i % 2, :], maxT[:, i % 2, :])
                if i == GROUP + 1:
                    q.wait(pool, "select", GROUP - 1, 2)
                    q.wait(dve, "b1 parts")
                    for t in range(GROUP):
                        row = PAD * t + BLOCKS
                        dma(b1_landed, select[row:row + PARTS, t, :], b1_parts[:].rearrange("o a n -> o (a n)"))
                g, phase = ffn_phase(i)
                if g is not None and phase >= 2:
                    t = (phase - 2) * 2
                    b = g * GROUP + t
                    q.wait(dve, "y", g, t + 1)
                    dma(y_stored[b // 2 % 2], out[b:b + 2].rearrange("b p d -> p b d"), y_out[:, b // 2 % 2])
            for n, semaphore in enumerate(y_stored):
                q.wait_semaphore(semaphore, 16 * len(range(n, N // 2, 2)))

        programs = ((pe, tensor_program), (act, scalar_program), (dve, vector_program),
                    (pool, pool_program), (sync, sync_program))
        for queue, program in programs:
            queue.begin(None, None)
            program(queue)
        block = ctx.enter_context(nc.Block())
        for (queue, program), place in zip(programs, (block.tensor, block.scalar, block.vector,
                                                      block.gpsimd, block.sync)):
            @place
            def _(engine, queue=queue, program=program):
                queue.begin(engine, queue.done)
                program(queue)


_INS = [("x", "x"), ("ctx", "ctx_1024"), ("g_xattn", "g_xattn"), ("g_ffn", "g_ffn"),
        ("w_router", "L0_ffn_w_router"), ("b_router", "L0_ffn_b_router"), ("w1T", "L0_ffn_w1"),
        ("b1", "L0_ffn_b1"), ("w2T", "L0_ffn_w2"), ("b2", "L0_ffn_b2")]


def kernel(**inputs):
    import concourse.bacc as bacc
    from concourse.bass_utils import run_bass_kernel_spmd

    nc = bacc.Bacc("TRN2", target_bir_lowering=False, num_devices=1)
    arrays, args = {}, []
    for name, key in _INS:
        a = np.asarray(inputs[key])
        a = np.ascontiguousarray(a.T if name in ("w1T", "w2T") else a)
        arrays[f"in_{name}"] = a
        args.append(nc.dram_tensor(f"in_{name}", a.shape, mybir.dt.from_np(a.dtype), kind="ExternalInput").ap())
    out = nc.dram_tensor("out_y", arrays["in_x"].shape, F32, kind="ExternalOutput").ap()
    build(nc, *args, out)
    r = run_bass_kernel_spmd(nc, [arrays], core_ids=[0])
    return r.results[0]["out_y"]
```

```python
from contextlib import ExitStack

import numpy as np

import concourse.bass as bass
from concourse import mybir

ALU = mybir.AluOpType
ACT = mybir.ActivationFunctionType
F32 = mybir.dt.float32
F32R = mybir.dt.float32r
BF16 = mybir.dt.bfloat16
AX_X = mybir.AxisListType.X

P = 128
HEADS = 16
SLOTS = 6
PARTS = 3
BANKS, BANK = 8, 512
GROUP = 4
PAIR = 2
PAD = 32
BLOCKS, TOP_K = 16, 4
LN_EPS = 1e-5
NEG = -(2.0 ** 126)
EXP_LOW = -87.33
TAKEN = -1.0e30
FILLER = 1.0e30

MADE = 4
Q_SLOTS = {"high": slice(0, 4, 3), "mid": slice(1, 2), "low": slice(2, 3)}
K_SLOTS = {"high": slice(0, 3, 2), "mid": slice(1, 2), "low": slice(3, 4)}
Q_REPEATED, K_REPEATED = 0, 1

LOAD_AHEAD = 5
FFN_LAG = 6


class Queue:

    def __init__(self):
        self.number = {}
        self.begin(None, None)

    def begin(self, engine, semaphore):
        self.engine, self.semaphore, self.count, self.waited = engine, semaphore, 0, {}

    def run(self, emit, *product):
        if product:
            self.count += 1
            self.number[product] = self.count
        if self.engine is not None:
            instruction = emit(self.engine)
            if product:
                instruction.then_inc(self.semaphore, 1)

    def wait(self, maker, *product):
        if self.engine is not None:
            self.wait_semaphore(maker.semaphore_of(), maker.number[product])

    def wait_semaphore(self, semaphore, value):
        if self.engine is not None and self.waited.get(semaphore.name, 0) < value:
            self.engine.wait_ge(semaphore, value)
            self.waited[semaphore.name] = value

    def settle(self):
        if self.count:
            self.wait_semaphore(self.done, self.count)

    def semaphore_of(self):
        return self.done


def build(nc, A_x, A_ctx, A_g_xattn, A_g_ffn, A_w_router, A_b_router, A_w1T, A_b1, A_w2T, A_b2, out):
    N, S, D = A_x.shape
    HID = A_w1T.shape[1]
    HD = D // HEADS
    BLOCK = HID // BLOCKS
    KC = D // P
    HC = HID // P
    STACK = SLOTS * HD
    MAX_ROW = STACK + 1
    HALF = S // 2
    GROUPS = N // GROUP
    HB = BANK // S
    HEAD_OF = [2 * n for n in range(HEADS // 2)] + [2 * n + 1 for n in range(HEADS // 2)]
    MADE_ROWS = MADE * HD
    PAIRS_S = HEADS // 2 * S
    VW = HD + 1
    SCALE = float(HD) ** -0.5
    assert S == P and N % GROUP == 0 and HEADS // HB == 4 and MAX_ROW + PARTS <= P and HC == 8 and 2 * MADE_ROWS == P

    ctx = ExitStack()
    with ctx:
        def sb(name, shape, dt):
            return ctx.enter_context(nc.sbuf_tensor(name, shape, dt))

        def sem(name):
            return ctx.enter_context(nc.semaphore(name))

        banks = [ctx.enter_context(nc.psum_tensor(f"bank{i}", [P, BANK], F32)) for i in range(BANKS)]

        ident = sb("ident", [P, P], F32)
        ident16 = sb("ident16", [P, P], BF16)
        causal = sb("causal", [P, HB, S], BF16)
        half_power = sb("half_power", [P, 1], F32)
        gates = sb("gates", [P, 2], F32)
        tanh_g = sb("tanh_g", [P, 2], F32)
        b2_all = sb("b2_all", [P, D], F32)
        gated_b2 = sb("gated_b2", [P, D], F32)
        br_all = sb("br_all", [P, BLOCKS], F32)
        w_router = sb("w_router", [P, KC, PAD], F32)
        w_stage = sb("w_stage", [P, KC * HID], F32)
        w1_high = sb("w1_high", [P, KC, HID], F32R)
        w1_low = sb("w1_low", [P, KC, HID], F32R)
        w2_high = sb("w2_high", [P, HC, D], F32R)
        w2_low = sb("w2_low", [P, HC, D], F32R)
        b1_parts = sb("b1_parts", [1, PARTS, HID], BF16)
        select = sb("select", [P, GROUP, HID], BF16)

        XS, CS, GS, VS = 8, 4, 8, 4
        x_in = sb("x_in", [P, XS, D], F32)
        c_in = sb("c_in", [P, CS, D], F32)
        stats1 = sb("stats1", [P, 2, 6], F32)
        mv1 = sb("mv1", [P, 2, 2], F32)
        ve1 = sb("ve1", [P, 2, 1], F32)
        rstd1 = sb("rstd1", [P, 2, 1], F32)
        qn = sb("qn", [P, 2, D], F32)
        q_rest = sb("q_rest", [P, 2, D], F32)
        k_rest = sb("k_rest", [P, 2, D], F32)
        q_stack = sb("q_stack", [P, 2, HEADS, MADE, HD], BF16)
        k_stack = sb("k_stack", [P, 2, HEADS, MADE, HD], BF16)
        v_ones = sb("v_ones", [P, VS, HEADS * VW + PAD - VW], F32)
        qT = sb("qT", [P, 2, HEADS * S], BF16)
        kT = sb("kT", [P, 2, HEADS * S], BF16)
        neg_max = sb("neg_max", [P, 2, HEADS], F32)
        max_rest = sb("max_rest", [P, 2, 2, HEADS], F32)
        max_parts = sb("max_parts", [P, 2, PARTS, HEADS], BF16)
        maxT = sb("maxT", [PARTS * HEADS, 2, S], BF16)
        weights = sb("weights", [P, 2, HEADS, S], F32)
        oT = sb("oT", [P, 2, BANK], F32)
        gain = sb("gain", [P, 2, 2, HEADS], F32)
        att = sb("att", [P, D], F32)
        x2 = sb("x2", [P, 2, D], F32)
        stats2 = sb("stats2", [P, 2, 6], F32)
        mv2 = sb("mv2", [P, 2, 2], F32)
        ve2 = sb("ve2", [P, 2, 1], F32)
        rstd2 = sb("rstd2", [P, 2, 1], F32)
        xn = sb("xn", [P, 2, D], F32)
        x2_b2 = sb("x2_b2", [P, GS, D], F32)

        xT = sb("xT", [P, KC, GROUP, S], F32)
        xT_high = sb("xT_high", [P, 2, KC, GROUP, S], F32R)
        xT_low = sb("xT_low", [P, 2, KC, GROUP, S], F32R)
        logitT = sb("logitT", [P, S], F32)
        logit = sb("logit", [P, GROUP, BLOCKS], F32)
        top8 = sb("top8", [P, GROUP, 8], F32)
        shifted = sb("shifted", [P, GROUP, BLOCKS], F32)
        below = sb("below", [P, GROUP, BLOCKS + 4], F32)
        chosen = sb("chosen", [P, GROUP, 8], F32)
        marked = sb("marked", [P, GROUP, BLOCKS + 4], F32)
        top_rest = sb("top_rest", [P, GROUP, TOP_K], F32)
        unused = sb("unused", [P, GROUP, PAD], BF16)
        unusedT = sb("unusedT", [P, 2, S], BF16)
        h_high = sb("h_high", [P, HC, GROUP * S], F32R)
        h_low = sb("h_low", [P, HC, GROUP * S], F32R)
        y_out = sb("y_out", [P, 2, 2, D], F32)

        b1_row = y_out[0:1].rearrange("p a b d -> p (a b d)")

        pe, act, dve, pool = (Queue() for _ in range(4))
        for queue, name in ((pe, "pe_done"), (act, "act_done"), (dve, "dve_done"), (pool, "pool_done")):
            queue.done = sem(name)
        sync = Queue()
        sync.done = sem("sync_done")
        x_landed = [sem(f"x_landed{i}") for i in range(XS // PAIR)]
        c_landed = [sem(f"c_landed{i}") for i in range(CS // PAIR)]
        gates_landed = sem("gates_landed")
        small_landed = sem("small_landed")
        w_landed = sem("w_landed")
        b1_landed = sem("b1_landed")
        q_landed = [sem(f"q_landed{i}") for i in range(2)]
        k_landed = [sem(f"k_landed{i}") for i in range(2)]
        max_landed = [sem(f"max_landed{i}") for i in range(2)]
        y_stored = [sem(f"y_stored{i}") for i in range(2)]

        def landed(semaphores, b):
            turn, n = divmod(b // PAIR, len(semaphores))
            return semaphores[n], 16 * (turn + 1)

        def stack_landed(semaphores, b):
            return semaphores[b % 2], 16 * (b // 2 + 1)

        def heads_of(odd):
            return slice(odd * PAIRS_S, (odd + 1) * PAIRS_S)

        def stack_evacuated(q, copy, side, b, odd):
            rows = qT if side == "q" else kT
            q.wait(pe, side + "T", b)
            if b >= 2:
                q.wait(pe, "shifted", b - 2, HEADS // HB - 1)
            bank = banks[bank_of[(side + "T", b)]][odd * MADE_ROWS:(odd + 1) * MADE_ROWS, :].bitcast(BF16)
            q.run(lambda e: copy(e)(rows[0:MADE_ROWS, b % 2, heads_of(odd)], bank), side + "T", b, odd)

        def heads_view(ap):
            return ap.rearrange("p (h d) -> p h d", d=HD)

        def weight_pieces(i):
            n, turn = divmod(i, 3)
            if n not in (0, 1) or turn == 2:
                return []
            high, low = ((w1_high, w1_low), (w2_high, w2_low))[n]
            high, low = (t[:].rearrange("p c n -> p (c n)") for t in (high, low))
            size = KC * HID // 4
            cols = [slice((2 * turn + m) * size, (2 * turn + m + 1) * size) for m in range(2)]
            return [(f"w{n + 1}", 2 * turn + m, w_stage[:, c], high[:, c], low[:, c]) for m, c in enumerate(cols)]

        def ffn_phase(i):
            g, phase = divmod(i - FFN_LAG, GROUP)
            return (g, phase) if 0 <= g < GROUPS else (None, None)

        def router_group(i):
            b = i - 2
            return b // GROUP if 0 <= b < N and b % GROUP == GROUP - 1 else None

        FIRST, LAST = -3, GROUP * (GROUPS - 1) + FFN_LAG + 3
        ITERATIONS = range(FIRST, LAST + 1)
        bank_of = {}

        def tensor_program(q):
            ring = []

            def take(name, *freed_by, also=None):
                n = len(ring)
                bank_of[name] = n % BANKS
                if n >= BANKS:
                    for last_read in ring[n - BANKS]:
                        q.wait(*last_read)
                ring.append((freed_by, also) if also else (freed_by,))
                return banks[n % BANKS]

            def mm(*product, **args):
                q.run(lambda e: e.matmul(**args), *product)

            def tr(out_, in_, identity, *product):
                q.run(lambda e: e.transpose(out_, in_, identity), *product)

            def stacks_transposed(b):
                s = b % 2
                for side, stack, maker, name in (("q", q_stack, dve, "q low"), ("k", k_stack, pool, "k low")):
                    q.wait(maker, name, b)
                    also = (dve, "qT", b, 0) if side == "q" else None
                    bank = take((side + "T", b), act, side + "T", b, 1, also=also)[:].bitcast(BF16)
                    for h in range(0, HEADS, 2):
                        last = (side + "T", b) if h == HEADS - 2 else ()
                        tr(bank[:, h // 2 * S:(h // 2 + 1) * S],
                           stack[:, s, h:h + 2].rearrange("p h s d -> p (h s d)"), ident16[:], *last)

            def scores(b):
                s = b % 2
                q.wait_semaphore(*stack_landed(q_landed, b))
                q.wait_semaphore(*stack_landed(k_landed, b))
                for u in range(HEADS // HB):
                    bank = take(("score", b, u), dve, "max", b, u)
                    for j in range(HB):
                        h = u * HB + j
                        cols = slice(h * S, (h + 1) * S)
                        mm(out=bank[:, j * S:(j + 1) * S], lhsT=qT[0:MAX_ROW, s, cols],
                           rhs=kT[0:MAX_ROW, s, cols], start=j == 0, stop=False)
                    per_head = bank[:].rearrange("p (h k) -> p h k", k=S)
                    for half in range(2):
                        own = slice(half * HALF, (half + 1) * HALF)
                        last = ("score", b, u) if half else ()
                        mm(*last, out=per_head[own, :, own], lhsT=ident16[:, own], rhs=causal[:, :, own],
                           start=False, stop=True, tile_position=(0, half * HALF))

            def max_transposed(b):
                s = b % 2
                q.wait(dve, "max low", b)
                bank = take(("maxT", b), dve, "maxT", b)[:].bitcast(BF16)
                tr(bank[0:PARTS * HEADS, 0:S], max_parts[:, s].rearrange("p a h -> p (a h)"),
                   ident16[:], "maxT", b)

            def shifted_scores(b):
                s = b % 2
                q.wait_semaphore(max_landed[s], 16 * (b // 2 + 1))
                for u in range(HEADS // HB):
                    bank = take(("shifted", b, u), act, "exp", b, u)
                    for j in range(HB):
                        h = u * HB + j
                        cols = slice(h * S, (h + 1) * S)
                        last = ("shifted", b, u) if j == HB - 1 else ()
                        mm(*last, out=bank[:, j * S:(j + 1) * S], lhsT=kT[0:MAX_ROW + PARTS, s, cols],
                           rhs=qT[0:MAX_ROW + PARTS, s, cols], start=True, stop=True)

            def attention_out(b):
                s, vs = b % 2, b % VS
                bank = take(("oT", b), act, "oT", b)
                q.wait(pool, "v", b)
                for g in range(HEADS // HB):
                    q.wait(pool, "causal", b, g // 2)
                    for j in range(HB):
                        n = g * HB + j
                        h = HEAD_OF[n]
                        last = ("oT", b) if n == HEADS - 1 else ()
                        mm(*last, out=bank[PAD * j:PAD * (j + 1), g * S:(g + 1) * S],
                           lhsT=v_ones[:, vs, h * VW:h * VW + PAD], rhs=weights[:, s, n, :],
                           start=True, stop=True, tile_position=(0, PAD * j))

            def out_transposed(b):
                s = b % 2
                bank = take(("o", b), dve, "att", b)
                q.wait(act, "oT", b)
                for g in range(HEADS // HB):
                    last = ("o", b) if g == HEADS // HB - 1 else ()
                    tr(bank[:, g * P:(g + 1) * P], oT[:, s, g * S:(g + 1) * S], ident[:], *last)

            def x_transposed(b):
                s = b % 2
                q.wait(dve, "xn", b)
                bank = take(("xT", b), act, "xT", b)
                for c in range(KC):
                    last = ("xT", b) if c == KC - 1 else ()
                    tr(bank[:, c * S:(c + 1) * S], xn[:, s, c * P:(c + 1) * P], ident[:], *last)

            def router_logits(g):
                bank = take(("logitT", g), act, "logitT", g)
                q.wait(act, "xT", g * GROUP + GROUP - 1)
                for c in range(KC):
                    for t in range(GROUP):
                        last = ("logitT", g) if c == KC - 1 and t == GROUP - 1 else ()
                        mm(*last, out=bank[PAD * t:PAD * (t + 1), 0:S], lhsT=w_router[:, c, :],
                           rhs=xT[:, c, t, :], start=c == 0, stop=c == KC - 1,
                           tile_position=(0, PAD * t))

            def logits_back(g):
                bank = take(("logit", g), dve, "logit", g)
                q.wait(act, "logitT", g)
                tr(bank[:, 0:P], logitT[:], ident[:], "logit", g)

            def unused_transposed(g):
                q.wait(dve, "unused", g)
                bank = take(("unusedT", g), dve, "unusedT", g)[:].bitcast(BF16)
                tr(bank[:, 0:S], unused[:].rearrange("p t e -> p (t e)"), ident16[:], "unusedT", g)

            def hidden(g, c):
                gs = g % 2
                cols = slice(c * P, (c + 1) * P)
                if c == 0:
                    q.wait(dve, "xT low", g * GROUP + GROUP - 1)
                    q.wait(pool, "w1 low", 3)
                bank = take(("hidden", g, c), dve, "h low", g, c)
                for k in range(KC):
                    high, low = (t[:, gs, k].rearrange("p t s -> p (t s)") for t in (xT_high, xT_low))
                    mm(out=bank[:], lhsT=w1_high[:, k, cols], rhs=high, start=k == 0, stop=False)
                    mm(out=bank[:], lhsT=w1_high[:, k, cols], rhs=low, start=False, stop=False)
                    mm(out=bank[:], lhsT=w1_low[:, k, cols], rhs=high, start=False, stop=False)
                if c == 0:
                    q.wait(dve, "unusedT", g)
                    q.wait(pool, "select", GROUP - 1, 2)
                    q.wait_semaphore(b1_landed, 16 * (1 + GROUP))
                for t in range(GROUP):
                    last = ("hidden", g, c) if t == GROUP - 1 else ()
                    mm(*last, out=bank[:, t * S:(t + 1) * S], lhsT=select[:, t, cols],
                       rhs=unusedT[:, gs, :], start=False, stop=t == GROUP - 1)

            def ffn_out(g, t, half):
                if half == 0:
                    take(("ffn", g, t), dve, "y", g, t)
                bank = banks[bank_of[("ffn", g, t)]]
                toks = slice(t * S, (t + 1) * S)
                if g == 0:
                    q.wait(pool, "w2 low", 3)
                for c in range(half * HC // 2, (half + 1) * HC // 2):
                    q.wait(dve, "h low", g, c)
                    a, z = c == 0, c == HC - 1
                    last = ("ffn", g, t) if z else ()
                    mm(out=bank[:, 0:D], lhsT=h_high[:, c, toks], rhs=w2_high[:, c, :], start=a, stop=False)
                    mm(out=bank[:, 0:D], lhsT=h_high[:, c, toks], rhs=w2_low[:, c, :], start=False, stop=False)
                    mm(*last, out=bank[:, 0:D], lhsT=h_low[:, c, toks], rhs=w2_high[:, c, :],
                       start=False, stop=z)

            def ffn_piece(i, n):
                g, phase = ffn_phase(i)
                if g is None:
                    return
                if phase < 2:
                    hidden(g, phase * 4 + n)
                else:
                    ffn_out(g, (phase - 2) * 2 + n // 2, n % 2)

            q.wait(pool, "identities")
            for i in ITERATIONS:
                if 0 <= i + 1 < N:
                    stacks_transposed(i + 1)
                ffn_piece(i, 0)
                if 0 <= i - 2 < N:
                    x_transposed(i - 2)
                ffn_piece(i, 1)
                if 0 <= i < N:
                    max_transposed(i)
                if 0 <= i - 1 < N:
                    attention_out(i - 1)
                g = router_group(i)
                if g is not None:
                    if g == 0:
                        q.wait_semaphore(small_landed, 16 * (KC + 2))
                    router_logits(g)
                if g is not None:
                    logits_back(g)
                if 0 <= i - 1 < N:
                    out_transposed(i - 1)
                ffn_piece(i, 2)
                ffn_piece(i, 3)
                if g is not None:
                    unused_transposed(g)
                if i + 1 == 0:
                    q.wait(pool, "causal mask")
                    q.wait(pool, "kT rows")
                    q.wait(dve, "qT rows")
                work = [(shifted_scores, i), (scores, i + 1)]
                for stage, b in work[::-1] if i < FFN_LAG - 1 else work:
                    if 0 <= b < N:
                        stage(b)

        def scalar_program(q):
            def cast(stack, slots, source, s):
                n = len(range(*slots.indices(SLOTS)))
                q_in = heads_view(source).unsqueeze(2).to_broadcast([P, HEADS, n, HD])
                return lambda e: e.copy(stack[:, s, :, slots, :], q_in)

            def q_cast(b, part):
                s = b % 2
                if part == "high":
                    q.wait(dve, "qn", b)
                    if b >= 2:
                        q.wait(pe, "qT", b - 2)
                    q.run(cast(q_stack, Q_SLOTS["high"], qn[:, s], s), "q high", b)
                else:
                    q.wait(dve, "q rest", b)
                    q.run(cast(q_stack, Q_SLOTS["mid"], q_rest[:, s], s), "q mid", b)

            def k_cast(b, part):
                s = b % 2
                if part == "high":
                    q.wait_semaphore(*landed(c_landed, b))
                    if b >= 2:
                        q.wait(pe, "kT", b - 2)
                    q.run(cast(k_stack, K_SLOTS["high"], c_in[:, b % CS], s), "k high", b)
                else:
                    q.wait(pool, "k rest", b)
                    q.run(cast(k_stack, K_SLOTS["mid"], k_rest[:, s], s), "k mid", b)

            def exponentials(b):
                s = b % 2
                if b >= 2:
                    q.wait(pe, "oT", b - 2)
                for u in range(HEADS // HB):
                    q.wait(pe, "shifted", b, u)
                    bank = banks[bank_of[("shifted", b, u)]]
                    q.run(lambda e: e.activation(
                        weights[:, s, u * HB:(u + 1) * HB, :].rearrange("p h q -> p (h q)"), bank[:],
                        ACT.Exp, scale=SCALE), "exp", b, u)

            def relu_high(g, c):
                q.wait(pe, "hidden", g, c)
                if g >= 1:
                    q.wait(pe, "ffn", g - 1, GROUP - 1)
                bank = banks[bank_of[("hidden", g, c)]]
                q.run(lambda e: e.activation(h_high[:, c, :], bank[:], ACT.Relu), "h high", g, c)

            def ffn_piece(i, n):
                g, phase = ffn_phase(i)
                if g is not None and phase < 2:
                    relu_high(g, phase * 4 + n)

            def weights_high(i):
                for name, m, stage, high, _ in weight_pieces(i):
                    q.wait_semaphore(w_landed, 16 if name == "w1" else 32)
                    q.run(lambda e: e.copy(high, stage), name + " high", m)
                if i == 2:
                    q.wait_semaphore(b1_landed, 16)
                    q.run(lambda e: e.copy(b1_parts[:, 0], b1_row), "b1 high")
                if i == 5:
                    q.wait(pool, "b1 rest")
                    q.run(lambda e: e.copy(b1_parts[:, 1], b1_row), "b1 mid")

            for i in ITERATIONS:
                if 0 <= i - 1 < N:
                    exponentials(i - 1)
                if 0 <= i + 1 < N:
                    stack_evacuated(q, lambda e: e.copy, "q", i + 1, 1)
                    stack_evacuated(q, lambda e: e.copy, "k", i + 1, 0)
                    stack_evacuated(q, lambda e: e.copy, "k", i + 1, 1)
                if 0 <= i + 2 < N:
                    k_cast(i + 2, "high")
                ffn_piece(i, 0)
                if 0 <= i - 2 < N:
                    b = i - 2
                    g, t = divmod(b, GROUP)
                    q.wait(pe, "xT", b)
                    if b >= GROUP:
                        q.wait(dve, "xT low", b - 1)
                        q.wait(pe, "logitT", g - 1)
                    bank = banks[bank_of[("xT", b)]]
                    q.run(lambda e: e.copy(xT[:, :, t, :], bank[:, 0:D].rearrange("p (c s) -> p c s", s=S)),
                          "xT", b)
                if 0 <= i + 2 < N:
                    q_cast(i + 2, "high")
                    k_cast(i + 2, "mid")
                ffn_piece(i, 1)
                if 0 <= i - 1 < N:
                    b = i - 1
                    q.wait(pe, "oT", b)
                    bank = banks[bank_of[("oT", b)]]
                    q.run(lambda e: e.copy(oT[:, b % 2, :], bank[:]), "oT", b)
                g = router_group(i)
                if g is not None:
                    q.wait(pe, "logitT", g)
                    bank = banks[bank_of[("logitT", g)]]
                    q.run(lambda e: e.copy(logitT[:], bank[:, 0:S]), "logitT", g)
                if 0 <= i + 2 < N:
                    q_cast(i + 2, "mid")
                ffn_piece(i, 2)
                ffn_piece(i, 3)
                weights_high(i)
                if i == 0:
                    q.wait_semaphore(gates_landed, 32)
                    q.run(lambda e: e.activation(tanh_g[:], gates[:], ACT.Tanh), "tanh")

        def vector_program(q):
            def constants():
                q.run(lambda e: e.memset(w_router[:], 0.0), "w_router zero")
                row = qT[STACK:MAX_ROW].rearrange("p s (h t) -> p (s h) t", t=S)
                q.run(lambda e: e.memset(row[:, :, 0:HALF], NEG))
                q.run(lambda e: e.memset(row[:, :, HALF:], 0.0), "qT rows")
                q.run(lambda e: e.memset(below[:, :, BLOCKS:], FILLER))
                q.run(lambda e: e.memset(chosen[:, :, TOP_K:], FILLER))
                q.run(lambda e: e.memset(unused[:], 0.0), "unused zero")
                q.wait(q, "unused zero")
                q.run(lambda e: e.memset(unused[:, :, BLOCKS:BLOCKS + PARTS], 1.0), "constants")
                q.wait(q, "constants")

            def stats_of(source, stats, mv, s, name, b):
                q.run(lambda e: e.bn_stats(stats[:, s, :], source), name + " stats", b)
                q.wait(q, name + " stats", b)
                q.run(lambda e: e.bn_aggr(mv[:, s, :], stats[:, s, :]), name + " mean", b)

            def layernorm_stats(b):
                q.wait_semaphore(*landed(x_landed, b))
                stats_of(x_in[:, b % XS, :], stats1, mv1, b % 2, "x", b)

            def normalised(b):
                s = b % 2
                q.wait(pool, "rstd1", b)
                q.run(lambda e: e.tensor_scalar(qn[:, s], x_in[:, b % XS, :], mv1[:, s, 0:1], rstd1[:, s],
                                                ALU.subtract, ALU.mult), "qn", b)

            def q_remainder(b):
                s = b % 2
                q.wait(act, "q high", b)
                q.run(lambda e: e.tensor_tensor(heads_view(q_rest[:, s]), heads_view(qn[:, s]),
                                                q_stack[:, s, :, 0, :], ALU.subtract), "q rest", b)

            def q_lowest(b):
                s = b % 2
                q.wait(act, "q mid", b)
                q.run(lambda e: e.tensor_tensor(q_stack[:, s, :, 2, :], heads_view(q_rest[:, s]),
                                                q_stack[:, s, :, 1, :], ALU.subtract), "q low", b)

            def row_maximum(b):
                s = b % 2
                for u in range(HEADS // HB):
                    q.wait(pe, "score", b, u)
                    bank = banks[bank_of[("score", b, u)]]
                    q.run(lambda e: e.tensor_reduce(
                        out=neg_max[:, s, u * HB:(u + 1) * HB], in_=bank[:].rearrange("p (h k) -> p h k", h=HB),
                        axis=AX_X, op=ALU.max, negate=True), "max", b, u)

            def maximum_parts(b):
                s = b % 2
                parts, rest = max_parts[:, s], max_rest[:, s]
                q.wait(q, "max", b, HEADS // HB - 1)
                if b >= 2:
                    q.wait(pe, "maxT", b - 2)
                q.run(lambda e: e.tensor_copy(parts[:, 0], neg_max[:, s]), "max high", b)
                q.wait(q, "max high", b)
                q.run(lambda e: e.tensor_tensor(rest[:, 0], neg_max[:, s], parts[:, 0], ALU.subtract), "max rest", b)
                q.wait(q, "max rest", b)
                q.run(lambda e: e.tensor_copy(parts[:, 1], rest[:, 0]), "max mid", b)
                q.wait(q, "max mid", b)
                q.run(lambda e: e.tensor_tensor(parts[:, 2], rest[:, 0], parts[:, 1], ALU.subtract), "max low", b)

            def maximum_rows(b):
                s = b % 2
                q.wait(pe, "maxT", b)
                if b >= 2:
                    q.wait_semaphore(max_landed[s], 16 * (b // 2))
                bank = banks[bank_of[("maxT", b)]][0:PARTS * HEADS, :].bitcast(BF16)
                q.run(lambda e: e.tensor_copy(maxT[:, s, :], bank[:, 0:S]), "maxT", b)

            def attention_added(b):
                s = b % 2
                q.wait(pe, "o", b)
                bank = banks[bank_of[("o", b)]][:].rearrange("p (h d) -> p h d", d=PAD)
                q.run(lambda e: e.reciprocal(gain[:, s, 0].unsqueeze(2), bank[:, :, HD:HD + 1]), "1/sum", b)
                q.wait(q, "1/sum", b)
                if b == 0:
                    q.wait(act, "tanh")
                q.run(lambda e: e.tensor_scalar(gain[:, s, 1], gain[:, s, 0], tanh_g[:, 0:1], None, ALU.mult),
                      "gain", b)
                q.wait(q, "gain", b)
                in_heads = att[:].rearrange("p (h o d) -> p o h d", o=2, d=HD)
                q.run(lambda e: e.tensor_tensor(
                    in_heads, bank[:, :, 0:HD].rearrange("p (o h) d -> p o h d", o=2),
                    gain[:, s, 1].rearrange("p (o h) -> p o h", o=2).unsqueeze(3)
                    .to_broadcast([P, 2, HEADS // 2, HD]), ALU.mult), "att", b)
                q.wait(q, "att", b)
                if b >= 2:
                    q.wait(pool, "x2 b2", b - 2)
                q.run(lambda e: e.tensor_tensor(x2[:, s], att[:], x_in[:, b % XS, :], ALU.add), "x2", b)
                q.wait(q, "x2", b)
                stats_of(x2[:, s], stats2, mv2, s, "x2", b)

            def normalised_again(b):
                s = b % 2
                q.wait(pool, "rstd2", b)
                if b >= 2:
                    q.wait(pe, "xT", b - 2)
                q.run(lambda e: e.tensor_scalar(xn[:, s], x2[:, s], mv2[:, s, 0:1], rstd2[:, s],
                                                ALU.subtract, ALU.mult), "xn", b)

            def x_parts(b):
                g, t = divmod(b, GROUP)
                gs = g % 2
                q.wait(act, "xT", b)
                if g >= 2 and t == 0:
                    q.wait(pe, "hidden", g - 2, HC - 1)
                q.run(lambda e: e.tensor_copy(xT_high[:, gs, :, t, :], xT[:, :, t, :]), "xT high", b)
                q.wait(q, "xT high", b)
                q.run(lambda e: e.tensor_tensor(xT_low[:, gs, :, t, :], xT[:, :, t, :],
                                                xT_high[:, gs, :, t, :].bitcast(F32), ALU.subtract), "xT low", b)

            def relu_low(g, c):
                q.wait(act, "h high", g, c)
                bank = banks[bank_of[("hidden", g, c)]]
                q.run(lambda e: e.scalar_tensor_tensor(h_low[:, c, :], bank[:], 0.0, h_high[:, c, :].bitcast(F32),
                                                       ALU.max, ALU.subtract), "h low", g, c)

            def finished(g, t):
                b = g * GROUP + t
                pair = b // 2
                q.wait(pe, "ffn", g, t)
                if b % 2 == 0 and pair >= 2:
                    q.wait_semaphore(y_stored[pair % 2], 16 * (pair // 2))
                if b == 0:
                    q.wait(act, "tanh")
                q.wait(pool, "x2 b2", b)
                bank = banks[bank_of[("ffn", g, t)]]
                q.run(lambda e: e.scalar_tensor_tensor(y_out[:, pair % 2, b % 2, :], bank[:, 0:D], tanh_g[:, 1:2],
                                                       x2_b2[:, b % GS, :], ALU.mult, ALU.add), "y", g, t)

            def ffn_piece(i, n):
                g, phase = ffn_phase(i)
                if g is None:
                    return
                if phase < 2:
                    relu_low(g, phase * 4 + n)
                elif n % 2:
                    finished(g, (phase - 2) * 2 + n // 2)

            def route(g):
                q.wait(pe, "logit", g)
                bank = banks[bank_of[("logit", g)]][:, 0:P].rearrange("p (t e) -> p t e", e=PAD)
                if g == 0:
                    q.wait_semaphore(small_landed, 16 * (KC + 2))
                q.run(lambda e: e.tensor_tensor(logit[:], bank[:, :, 0:BLOCKS],
                                                br_all[:].unsqueeze(1).to_broadcast([P, GROUP, BLOCKS]), ALU.add),
                      "logit", g)
                q.wait(q, "logit", g)
                for t in range(GROUP):
                    q.run(lambda e: e.max(top8[:, t, :], logit[:, t, :]), "top8", g, t)
                q.wait(q, "top8", g, GROUP - 1)
                largest = top8[:, :, 0:1]
                q.run(lambda e: e.tensor_tensor(shifted[:], logit[:], largest.to_broadcast([P, GROUP, BLOCKS]),
                                                ALU.subtract), "shifted", g)
                q.run(lambda e: e.tensor_tensor(top_rest[:], top8[:, :, 0:TOP_K],
                                                largest.to_broadcast([P, GROUP, TOP_K]), ALU.subtract), "top rest", g)
                q.wait(q, "shifted", g)
                q.run(lambda e: e.tensor_scalar(below[:, :, 0:BLOCKS], shifted[:], EXP_LOW, None, ALU.max), "below", g)
                q.wait(q, "top rest", g)
                q.run(lambda e: e.tensor_scalar(chosen[:, :, 0:TOP_K], top_rest[:], EXP_LOW, None, ALU.max),
                      "chosen", g)
                q.wait(q, "chosen", g)
                for t in range(GROUP):
                    q.run(lambda e: e.match_replace(out=marked[:, t, :], in_to_replace=chosen[:, t, :],
                                                    in_values=below[:, t, :], imm_value=TAKEN), "marked", g, t)
                q.wait(q, "marked", g, GROUP - 1)
                q.run(lambda e: e.tensor_scalar(unused[:, :, 0:BLOCKS], marked[:, :, 0:BLOCKS], TAKEN, -1.0,
                                                ALU.is_equal, ALU.add), "unused", g)

            q.run(lambda e: e.memset(half_power[:], -0.5), "half_power")
            constants()
            for i in ITERATIONS:
                if 0 <= i < N:
                    row_maximum(i)
                    maximum_parts(i)
                if 0 <= i + 1 < N:
                    stack_evacuated(q, lambda e: e.tensor_copy, "q", i + 1, 0)
                if 0 <= i + 3 < N:
                    layernorm_stats(i + 3)
                if 0 <= i + 2 < N:
                    normalised(i + 2)
                if 0 <= i - 2 < N:
                    x_parts(i - 2)
                ffn_piece(i, 0)
                if 0 <= i + 2 < N:
                    q_remainder(i + 2)
                ffn_piece(i, 1)
                if 0 <= i < N:
                    maximum_rows(i)
                g = router_group(i)
                if g is not None:
                    route(g)
                if 0 <= i - 1 < N:
                    attention_added(i - 1)
                if 0 <= i + 2 < N:
                    q_lowest(i + 2)
                ffn_piece(i, 2)
                if 0 <= i - 1 < N:
                    normalised_again(i - 1)
                ffn_piece(i, 3)
                if g is not None:
                    q.wait(pe, "unusedT", g)
                    bank = banks[bank_of[("unusedT", g)]][:].bitcast(BF16)
                    q.run(lambda e: e.tensor_copy(unusedT[:, g % 2, :], bank[:, 0:S]), "unusedT", g)
                if i == 1:
                    q.wait_semaphore(small_landed, 16 * (KC + 2))
                    q.wait(act, "tanh")
                    q.run(lambda e: e.tensor_scalar(gated_b2[:], b2_all[:], tanh_g[:, 1:2], None, ALU.mult), "gated b2")

        def pool_program(q):
            def rstd(mv, ve, result, s, maker_name, name, b):
                q.wait(dve, maker_name, b)
                q.run(lambda e: e.tensor_scalar(ve[:, s], mv[:, s, 1:2], LN_EPS, None, ALU.add), name + " ve", b)
                q.wait(q, name + " ve", b)
                q.run(lambda e: e.tensor_tensor(result[:, s], ve[:, s], half_power[:], ALU.pow), name, b)

            def k_remainder(b):
                s = b % 2
                q.wait(act, "k high", b)
                q.run(lambda e: e.tensor_tensor(heads_view(k_rest[:, s]), heads_view(c_in[:, b % CS, :]),
                                                k_stack[:, s, :, 0, :], ALU.subtract), "k rest", b)

            def k_lowest(b):
                s = b % 2
                q.wait(act, "k mid", b)
                q.run(lambda e: e.tensor_tensor(k_stack[:, s, :, 3, :], heads_view(k_rest[:, s]),
                                                k_stack[:, s, :, 1, :], ALU.subtract), "k low", b)

            def values(b):
                q.wait_semaphore(*landed(c_landed, b))
                if b >= VS:
                    q.wait(pe, "oT", b - VS)
                v = v_ones[:, b % VS, 0:HEADS * VW].rearrange("p (h w) -> p h w", w=VW)
                q.run(lambda e: e.tensor_copy(v[:, :, 0:HD], heads_view(c_in[:, b % CS, :])), "v", b)

            def causal_weights(b):
                s = b % 2
                for half in range(2):
                    w = weights[:, s, half * 2 * HB:(half + 1) * 2 * HB, :]
                    q.wait(act, "exp", b, half * 2 + 1)
                    q.run(lambda e: e.affine_select(out=w, in_=w, compare_op=ALU.is_ge, fill=0.0, base=0,
                                                    pattern=[[0, 2 * HB], [1, S]], channel_multiplier=-1),
                          "causal", b, half)

            def identity(tile, name):
                q.run(lambda e: e.memset(tile[:], 0.0), name + " zero")
                q.wait(q, name + " zero")
                q.run(lambda e: e.affine_select(out=tile[:], in_=tile[:], compare_op=ALU.not_equal, fill=1.0,
                                                base=0, pattern=[[-1, P]], channel_multiplier=1), name)

            def causal_mask():
                q.run(lambda e: e.memset(causal[:], 0.0), "causal zero")
                q.wait(q, "causal zero")
                q.run(lambda e: e.affine_select(out=causal[:], in_=causal[:], compare_op=ALU.is_ge, fill=NEG,
                                                base=0, pattern=[[0, HB], [-1, S]], channel_multiplier=1),
                      "causal mask")

            def select_table(t):
                rows = select[PAD * t:PAD * (t + 1), t, :]
                q.run(lambda e: e.memset(rows, -NEG), "select", t, 0)
                q.wait(q, "select", t, 0)
                q.run(lambda e: e.affine_select(out=rows, in_=rows, compare_op=ALU.is_ge, fill=0.0, base=0,
                                                pattern=[[1, HID]], channel_multiplier=-BLOCK), "select", t, 1)
                q.wait(q, "select", t, 1)
                q.run(lambda e: e.affine_select(out=rows, in_=rows, compare_op=ALU.is_ge, fill=0.0,
                                                base=BLOCK - 1, pattern=[[-1, HID]], channel_multiplier=BLOCK),
                      "select", t, 2)

            def weights_low(i):
                for name, m, stage, high, low in weight_pieces(i):
                    q.wait(act, name + " high", m)
                    q.run(lambda e: e.tensor_tensor(low, stage, high.bitcast(F32), ALU.subtract), name + " low", m)
                if i == 4:
                    q.wait(act, "b1 high")
                    q.run(lambda e: e.tensor_tensor(b1_row, b1_row, b1_parts[:, 0], ALU.subtract), "b1 rest")
                if i == 5:
                    q.wait(act, "b1 mid")
                    q.run(lambda e: e.tensor_tensor(b1_parts[:, 2], b1_row, b1_parts[:, 1], ALU.subtract),
                          "b1 parts")

            identity(ident16, "ident16")
            identity(ident, "identities")
            q.run(lambda e: e.memset(v_ones[:, :, HEADS * VW:], 0.0), "v padding")
            for s in range(VS):
                ones = v_ones[:, s, 0:HEADS * VW].rearrange("p (h w) -> p h w", w=VW)[:, :, HD:VW]
                q.run(lambda e: e.memset(ones, 1.0), "v ones", s)
            q.settle()
            q.run(lambda e: e.memset(kT[STACK:MAX_ROW + PARTS, :, :], 1.0), "kT ones")
            q.settle()
            row = kT[STACK:MAX_ROW].rearrange("p s (h t) -> p (s h) t", t=S)
            q.run(lambda e: e.memset(row[:, :, 0:HALF], 0.0), "kT rows")
            q.settle()
            for i in ITERATIONS:
                if 0 <= i - 1 < N:
                    causal_weights(i - 1)
                if 0 <= i + 3 < N:
                    if i + 3 == 0:
                        q.wait(dve, "half_power")
                    rstd(mv1, ve1, rstd1, (i + 3) % 2, "x mean", "rstd1", i + 3)
                if 0 <= i + 2 < N:
                    k_remainder(i + 2)
                    values(i + 2)
                    k_lowest(i + 2)
                if 0 <= i - 1 < N:
                    b = i - 1
                    rstd(mv2, ve2, rstd2, b % 2, "x2 mean", "rstd2", b)
                    if b == 0:
                        q.wait(dve, "gated b2")
                    if b >= GS:
                        q.wait(dve, "y", *divmod(b - GS, GROUP))
                    q.run(lambda e: e.tensor_tensor(x2_b2[:, b % GS, :], x2[:, b % 2], gated_b2[:], ALU.add),
                          "x2 b2", b)
                if i == -1:
                    causal_mask()
                if i == 0:
                    q.run(lambda e: e.memset(select[:], 0.0), "select zero")
                    q.wait(q, "select zero")
                if 0 <= i < GROUP:
                    q.settle()
                    select_table(i)
                    q.settle()
                weights_low(i)

        def sync_program(q):
            def dma(semaphore, dst, src):
                q.run(lambda e: e.dma_start(dst, src).then_inc(semaphore, 16))

            def load(n):
                tiles = slice(n * PAIR, (n + 1) * PAIR)
                xs, cs = n % (XS // PAIR), n % (CS // PAIR)
                if n * PAIR >= CS:
                    b = n * PAIR - CS + PAIR - 1
                    q.wait(pool, "k rest", b)
                    q.wait(pool, "v", b)
                dma(c_landed[cs], c_in[:, cs * PAIR:(cs + 1) * PAIR, :], A_ctx[tiles].rearrange("b p d -> p b d"))
                if n * PAIR >= XS:
                    q.wait(dve, "x2", n * PAIR - XS + PAIR - 1)
                dma(x_landed[xs], x_in[:, xs * PAIR:(xs + 1) * PAIR, :], A_x[tiles].rearrange("b p d -> p b d"))

            def rows_repeated(b):
                s = b % 2
                for side, rows, semaphore, first in (("q", qT, q_landed[s], Q_REPEATED * HD),
                                                     ("k", kT, k_landed[s], K_REPEATED * HD)):
                    q.wait(dve if side == "q" else act, side + "T", b, 0)
                    q.wait(act, side + "T", b, 1)
                    dma(semaphore, rows[MADE_ROWS:STACK, s, :], rows[first:first + STACK - MADE_ROWS, s, :])

            load(0)
            dma(gates_landed, gates[:, 0:1], A_g_xattn.partition_broadcast(P))
            dma(gates_landed, gates[:, 1:2], A_g_ffn.partition_broadcast(P))
            dma(small_landed, b2_all[:], A_b2.partition_broadcast(P))
            dma(small_landed, br_all[:], A_b_router.partition_broadcast(P))
            dma(b1_landed, b1_row, A_b1.rearrange("(o n) -> o n", o=1))
            q.wait(dve, "w_router zero")
            for c in range(KC):
                dma(small_landed, w_router[:, c, 0:BLOCKS], A_w_router[c * P:(c + 1) * P, :])
            load(1)
            dma(w_landed, w_stage[:].rearrange("p (c n) -> p c n", c=KC), A_w1T.rearrange("(c p) n -> p c n", p=P))
            for i in ITERATIONS:
                if i == 2:
                    q.wait(pool, "w1 low", 3)
                    dma(w_landed, w_stage[:].rearrange("p (c n) -> p c n", c=HC),
                        A_w2T.rearrange("(c p) n -> p c n", p=P))
                if 0 <= i + 1 < N:
                    rows_repeated(i + 1)
                if 0 <= i < N:
                    q.wait(dve, "maxT", i)
                    dma(max_landed[i % 2], qT[MAX_ROW:MAX_ROW + PARTS, i % 2, :], maxT[:, i % 2, :])
                b = i + LOAD_AHEAD
                if b >= 2 * PAIR and b % PAIR == 0 and b < N:
                    load(b // PAIR)
                if i == GROUP + 1:
                    q.wait(pool, "select", GROUP - 1, 2)
                    q.wait(pool, "b1 parts")
                    for t in range(GROUP):
                        row = PAD * t + BLOCKS
                        dma(b1_landed, select[row:row + PARTS, t, :], b1_parts[:].rearrange("o a n -> o (a n)"))
                g, phase = ffn_phase(i)
                if g is not None and phase >= 2:
                    t = (phase - 2) * 2
                    b = g * GROUP + t
                    q.wait(dve, "y", g, t + 1)
                    dma(y_stored[b // 2 % 2], out[b:b + 2].rearrange("b p d -> p b d"), y_out[:, b // 2 % 2])
            for n, semaphore in enumerate(y_stored):
                q.wait_semaphore(semaphore, 16 * len(range(n, N // 2, 2)))

        programs = ((pe, tensor_program), (act, scalar_program), (dve, vector_program),
                    (pool, pool_program), (sync, sync_program))
        for queue, program in programs:
            queue.begin(None, None)
            program(queue)
        block = ctx.enter_context(nc.Block())
        for (queue, program), place in zip(programs, (block.tensor, block.scalar, block.vector,
                                                      block.gpsimd, block.sync)):
            @place
            def _(engine, queue=queue, program=program):
                queue.begin(engine, queue.done)
                program(queue)


_INS = [("x", "x"), ("ctx", "ctx_1024"), ("g_xattn", "g_xattn"), ("g_ffn", "g_ffn"),
        ("w_router", "L0_ffn_w_router"), ("b_router", "L0_ffn_b_router"), ("w1T", "L0_ffn_w1"),
        ("b1", "L0_ffn_b1"), ("w2T", "L0_ffn_w2"), ("b2", "L0_ffn_b2")]


def kernel(**inputs):
    import concourse.bacc as bacc
    from concourse.bass_utils import run_bass_kernel_spmd

    nc = bacc.Bacc("TRN2", target_bir_lowering=False, num_devices=1)
    arrays, args = {}, []
    for name, key in _INS:
        a = np.asarray(inputs[key])
        a = np.ascontiguousarray(a.T if name in ("w1T", "w2T") else a)
        arrays[f"in_{name}"] = a
        args.append(nc.dram_tensor(f"in_{name}", a.shape, mybir.dt.from_np(a.dtype), kind="ExternalInput").ap())
    out = nc.dram_tensor("out_y", arrays["in_x"].shape, F32, kind="ExternalOutput").ap()
    build(nc, *args, out)
    r = run_bass_kernel_spmd(nc, [arrays], core_ids=[0])
    return r.results[0]["out_y"]
```
